# Optimizing a Trainium2 kernel written in Bass

```python
import numpy as np
import jax
import jax.numpy as jnp

def _softmax(x, axis=-1):
    return jax.nn.softmax(x, axis=axis)

def _gelu(x):
    return jax.nn.gelu(x, approximate=True)

def _silu(x):
    return jax.nn.silu(x)

def _sigmoid(x):
    return jax.nn.sigmoid(x)

def _layernorm(x, axis=-1, eps=1e-05):
    m = jnp.mean(x, axis=axis, keepdims=True)
    v = jnp.var(x, axis=axis, keepdims=True)
    return (x - m) / jnp.sqrt(v + eps)

def _scatter_add(tgt, idx, src, axis=0):
    return tgt.at[idx].add(src)

def _segment_sum(src, seg, n):
    return jax.ops.segment_sum(src, seg, n)
kernel_name = 'mk_cond_resid_d1_seqx_r2_9ccacd'

def setup_inputs(seed: int=0):
    np.random.seed(seed)
    _w = jnp.asarray

    def _rec_inputs():
        import jax
        import jax.numpy as jnp
        _rk = jax.random.key(seed)
        x = -0.000125 + 0.9999 * jax.random.normal(jax.random.fold_in(_rk, 1), (4, 1024, 512), jnp.float32)
        _lenS = 1024 - jax.random.randint(jax.random.fold_in(_rk, 7), (4,), 0, max(1, 1024 // 4) + 1, jnp.int32)
        _lenS2 = 1024 - jax.random.randint(jax.random.fold_in(_rk, 8), (4,), 0, max(1, 1024 // 4) + 1, jnp.int32)
        cond_1024 = 0.00782532 + 1.00527 * jax.random.normal(jax.random.fold_in(_rk, 11), (4, 512), jnp.float32)
        return (x, cond_1024)
    x, cond_1024 = _rec_inputs()

    def _L0_cond_setup():
        import jax, jax.numpy as jnp
        import numpy as np
        NHID = 512
        NHEAD = 16
        HEAD_DIM = 64
        B, L = (8, 2048)
        key = jax.random.key(seed)
        ks = jax.random.split(key, 12)
        s_in = 1.0 / np.sqrt(NHID)
        s_o = 1.0 / np.sqrt(NHEAD * HEAD_DIM)
        return {'x': jax.random.normal(ks[0], (B, L, NHID), dtype=jnp.float32), 'ax': jax.random.normal(ks[1], (B, NHID), dtype=jnp.float32), 'WQ_w': jax.random.normal(ks[2], (NHID, NHEAD * HEAD_DIM), dtype=jnp.float32) * s_in, 'WQ_b': jnp.zeros((NHEAD * HEAD_DIM,), dtype=jnp.float32), 'WK_w': jax.random.normal(ks[3], (NHID, NHEAD * HEAD_DIM), dtype=jnp.float32) * s_in, 'WK_b': jnp.zeros((NHEAD * HEAD_DIM,), dtype=jnp.float32), 'WV_w': jax.random.normal(ks[4], (NHID, NHEAD * HEAD_DIM), dtype=jnp.float32) * s_in, 'WV_b': jnp.zeros((NHEAD * HEAD_DIM,), dtype=jnp.float32), 'WO_w': jax.random.normal(ks[5], (NHEAD * HEAD_DIM, NHID), dtype=jnp.float32) * s_o, 'WO_b': jnp.zeros((NHID,), dtype=jnp.float32)}
    _L0_cond_all = _L0_cond_setup()
    _L0_cond_in = {k: v for k, v in _L0_cond_all.items() if k in ('WQ_w', 'WQ_b', 'WK_w', 'WK_b', 'WV_w', 'WV_b', 'WO_w', 'WO_b')}
    del _L0_cond_all
    return {'x': x, 'cond_1024': cond_1024, 'L0_cond_WQ_w': _L0_cond_in['WQ_w'], 'L0_cond_WQ_b': _L0_cond_in['WQ_b'], 'L0_cond_WK_w': _L0_cond_in['WK_w'], 'L0_cond_WK_b': _L0_cond_in['WK_b'], 'L0_cond_WV_w': _L0_cond_in['WV_w'], 'L0_cond_WV_b': _L0_cond_in['WV_b'], 'L0_cond_WO_w': _L0_cond_in['WO_w'], 'L0_cond_WO_b': _L0_cond_in['WO_b']}

def reference(x, cond_1024, L0_cond_WQ_w, L0_cond_WQ_b, L0_cond_WK_w, L0_cond_WK_b, L0_cond_WV_w, L0_cond_WV_b, L0_cond_WO_w, L0_cond_WO_b):
    import jax
    import jax.numpy as jnp

    def _L0_cond_ref(x, ax, WQ_w, WQ_b, WK_w, WK_b, WV_w, WV_b, WO_w, WO_b):
        import jax, jax.numpy as jnp
        import numpy as np
        NHID = 512
        NHEAD = 16
        HEAD_DIM = 64
        B, L = (8, 2048)
        Bx, Lx, H = x.shape
        nh, d = (NHEAD, HEAD_DIM)
        q = (x @ WQ_w + WQ_b).reshape(Bx, Lx, nh, d)
        k = (x @ WK_w + WK_b).reshape(Bx, Lx, nh, d)
        ak = (ax @ WK_w + WK_b).reshape(Bx, 1, nh, d)
        av = (ax @ WV_w + WV_b).reshape(Bx, 1, nh, d)
        pad_k = jnp.pad(k, ((0, 0), (1, 1), (0, 0), (0, 0)))
        k_shift = jnp.stack([pad_k[:, t:Lx + t] for t in range(3)], axis=3)
        akb = jnp.broadcast_to(ak, (Bx, Lx, nh, d))[:, :, :, None, :]
        avb = jnp.broadcast_to(av, (Bx, Lx, nh, d))[:, :, :, None, :]
        K = jnp.concatenate([akb, k_shift], axis=3)
        V = jnp.concatenate([avb, k_shift], axis=3)
        scores = jnp.einsum('blhd,blhjd->blhj', q, K) / jnp.sqrt(jnp.float32(d))
        alphas = jax.nn.softmax(scores, axis=-1)
        att = jnp.einsum('blhj,blhjd->blhd', alphas, V).reshape(Bx, Lx, nh * d)
        return att @ WO_w + WO_b
    x = x + _L0_cond_ref(x, cond_1024, L0_cond_WQ_w, L0_cond_WQ_b, L0_cond_WK_w, L0_cond_WK_b, L0_cond_WV_w, L0_cond_WV_b, L0_cond_WO_w, L0_cond_WO_b)
    return x

_drawn_inputs = setup_inputs


def setup_inputs(seed=0):
    import zlib

    import numpy as np

    out = dict(_drawn_inputs(seed))
    spreads = {'L0_cond_WQ_b': (0.0, 0.1),
     'L0_cond_WK_b': (0.0, 0.1),
     'L0_cond_WV_b': (0.0, 0.301),
     'L0_cond_WO_b': (0.0, 0.1)}
    factors = {}
    for name, (base, spread) in spreads.items():
        noise = np.random.default_rng([zlib.crc32(name.encode()), seed]).standard_normal(out[name].shape)
        drawn = base * np.exp(spread * noise) if base else spread * noise
        out[name] = jnp.asarray(drawn.astype(out[name].dtype))
    for name, factor in factors.items():
        out[name] = (out[name] * factor).astype(out[name].dtype)
    return out
```

```python
from contextlib import ExitStack

import concourse.bass as bass
from concourse import mybir

F32 = mybir.dt.float32
F32R = mybir.dt.float32r
ALU = mybir.AluOpType
ACT = mybir.ActivationFunctionType
AX = mybir.AxisListType

P = 128
C = 512
HEADS = 16
HD = 64
CH = HEADS * HD
CK = C // P
HK = CH // P
HALF = 512
TILES = 32
SLOTS = 4
SCALE = HD ** -0.5
TAPS = 4
AUX = TAPS - 1


def build(nc, xT, x, condT, wq, wk, wv, wo, bqk, bv, bo, ident_in, masks_in, out):
    with ExitStack() as ctx:
        def sb(name, shape, dt=F32):
            return ctx.enter_context(nc.sbuf_tensor(name, shape, dt))

        def ps(name, shape):
            return ctx.enter_context(nc.psum_tensor(name, shape, F32))

        def sem(name):
            return ctx.enter_context(nc.semaphore(name))

        wk_hi, wk_lo = sb("wk_hi", [P, CK, CH], F32R), sb("wk_lo", [P, CK, CH], F32R)
        wq_hi, wq_lo = sb("wq_hi", [P, CK, CH], F32R), sb("wq_lo", [P, CK, CH], F32R)
        wo_hi, wo_lo = sb("wo_hi", [P, HK, C], F32R), sb("wo_lo", [P, HK, C], F32R)
        products = sb("products", [P, TAPS, CH])
        weighted = sb("weighted", [P, TAPS, CH])
        keys = sb("keys", [P, SLOTS, CH])
        aux_key = sb("aux_key", [P, CH])
        aux_value = sb("aux_value", [P, CH])
        att = sb("att", [P, CH])
        attT_hi, attT_lo = sb("attT_hi", [P, HK, P], F32R), sb("attT_lo", [P, HK, P], F32R)
        xT_raw = sb("xT_raw", [P, 2, CK, P])
        xT_hi, xT_lo = sb("xT_hi", [P, SLOTS, CK, P], F32R), sb("xT_lo", [P, SLOTS, CK, P], F32R)
        cond_raw = sb("cond_raw", [P, CK, P])
        resid = sb("resid", [P, 2, C])
        out_sb = sb("out_sb", [P, 2, C])
        bo_rows = sb("bo_rows", [P, C])
        ident = sb("ident", [P, P])
        masks = sb("masks", [2, 3, P], F32R)
        low_row = sb("low_row", [2, 1])
        bias = sb("bias", [2, 2, CH], F32R)
        scores = sb("scores", [P, TAPS, HEADS])
        peak = sb("peak", [P, HEADS])
        shifted = sb("shifted", [P, TAPS, HEADS])
        expd = sb("expd", [P, TAPS, HEADS])
        total = sb("total", [P, HEADS])
        inverse = sb("inverse", [P, HEADS])
        alpha = sb("alpha", [P, TAPS, HEADS])
        bqk_raw = keys[0:2, 2:4, :]
        bqk_high = keys[0:2, 0:2, :]
        bv_row = att[0:1, :]
        masks_raw = aux_value[0:2, 0:3 * P].rearrange("q (m n) -> q m n", m=3)
        ones_row = masks_raw[0:1, 0, :]
        cond_hi, cond_lo = xT_hi[:, 3], xT_lo[:, 3]

        ps_k = ps("ps_k", [P, CH])
        ps_q = ps("ps_q", [P, CH])
        ps_t = ps("ps_t", [P, HK, P])
        ps_o = ps("ps_o", [P, C])

        wk_in = [sem(f"wk_in{c}") for c in range(CK)]
        wq_in = [sem(f"wq_in{c}") for c in range(CK)]
        wv_in = sem("wv_in")
        wo_in = [sem(f"wo_in{c}") for c in range(CK)]
        small_in = sem("small_in")
        late_in = sem("late_in")
        cond_in = sem("cond_in")
        xT_in = [sem(f"xT_in{s}") for s in range(2)]
        resid_in = [sem(f"resid_in{s}") for s in range(2)]
        stored = [sem(f"stored{s}") for s in range(2)]
        w_hi_ready = sem("w_hi_ready")
        w_lo_ready = sem("w_lo_ready")
        wo_lo_ready = sem("wo_lo_ready")
        bias_hi_ready = sem("bias_hi_ready")
        masks_ready = sem("masks_ready")
        bias_ready = sem("bias_ready")
        rows_set = sem("rows_set")
        cond_hi_ready = sem("cond_hi_ready")
        cond_ready = sem("cond_ready")
        x_hi_ready = sem("x_hi_ready")
        x_ready = sem("x_ready")
        k_half_done = sem("k_half_done")
        k_ready = sem("k_ready")
        av_done = sem("av_done")
        av_ready = sem("av_ready")
        q_done = sem("q_done")
        q_used = sem("q_used")
        scores_ready = sem("scores_ready")
        peak_ready = sem("peak_ready")
        shifted_ready = sem("shifted_ready")
        exp_ready = sem("exp_ready")
        total_ready = sem("total_ready")
        inverse_ready = sem("inverse_ready")
        alpha_ready = sem("alpha_ready")
        weighted_ready = sem("weighted_ready")
        aux_weighted = sem("aux_weighted")
        pair_summed = sem("pair_summed")
        att_ready = sem("att_ready")
        attT_done = sem("attT_done")
        attT_hi_ready = sem("attT_hi_ready")
        attT_ready = sem("attT_ready")
        resid_ready = sem("resid_ready")
        o_done = sem("o_done")
        out_ready = sem("out_ready")

        block = ctx.enter_context(nc.Block())

        def pipeline(eng, step, last):
            for t in range(SLOTS):
                step(0, t)
            with eng.Fori(1, TILES // SLOTS - 1) as i:
                for r in range(SLOTS):
                    step(i, r)
            for t in range(TILES - SLOTS, last + 1):
                step(*divmod(t, SLOTS))

        def bcast_heads(row):
            return row.unsqueeze(2).to_broadcast([P, HEADS, HD])

        def by_head(row):
            return row.rearrange("p (h d) -> p h d", h=HEADS)

        @block.sync
        def _(sp):
            def load_x(u, slot):
                sp.dma_start(xT_raw[:, slot], xT[u]).then_inc(xT_in[slot], 16)

            sp.dma_start(xT_raw[:, 0], xT[0]).then_inc(xT_in[0], 16)
            for c in range(CK):
                sp.dma_start(products[:, c, :], wk[:, c, :]).then_inc(wk_in[c], 16)
            sp.dma_start(bqk_raw, bqk).then_inc(small_in, 16)
            sp.dma_start(masks_raw, masks_in).then_inc(small_in, 16)
            sp.dma_start(xT_raw[:, 1], xT[1]).then_inc(xT_in[1], 16)
            sp.dma_start(cond_raw[:], condT).then_inc(cond_in, 16)
            for c in range(CK):
                sp.dma_start(weighted[:, c, :], wq[:, c, :]).then_inc(wq_in[c], 16)
            sp.wait_ge(x_ready, 1)
            load_x(2, 0)
            sp.dma_start(bv_row, bv).then_inc(late_in, 16)
            sp.dma_start(bo_rows[:], bo).then_inc(late_in, 16)
            sp.dma_start(ident[:], ident_in).then_inc(late_in, 16)
            sp.wait_ge(w_hi_ready, CK)
            sp.wait_ge(w_lo_ready, CK)
            sp.dma_start(products[:], wv).then_inc(wv_in, 16)
            sp.wait_ge(x_ready, 2)
            load_x(3, 1)
            sp.wait_ge(w_hi_ready, 2 * CK)
            sp.wait_ge(w_lo_ready, 2 * CK)
            for c in range(CK):
                sp.dma_start(weighted[:, c, :], wo[:, c, :]).then_inc(wo_in[c], 16)

            def step(i, r):
                t, static = i * SLOTS + r, isinstance(i, int)
                if not (static and t + 4 > TILES + 1):
                    sp.wait_ge(x_ready, t + 3)
                    load_x(t + 4, r % 2)
                if not (static and t < 3):
                    sp.wait_ge(out_ready, t - 2)
                    sp.dma_start(out[:, t - 3, :], out_sb[:, (r + 1) % 2, :]).then_inc(stored[(r + 1) % 2], 16)
                if not (static and not 1 <= t <= TILES):
                    sp.dma_start(resid[:, (r + 1) % 2, :], x[:, t - 1, :]).then_inc(resid_in[(r + 1) % 2], 16)

            pipeline(sp, step, TILES + 2)
            for s in range(2):
                sp.wait_ge(stored[s], 16 * (TILES // 2))

        @block.tensor
        def _(pe):
            def three_passes(dst, hi, lo, w_hi, w_lo, last):
                for lhs, rhs, stop in ((hi, w_hi, False), (hi, w_lo, False), (lo, w_hi, last)):
                    mm = pe.matmul(dst, lhs, rhs, start=False, stop=stop)
                return mm

            def keys_of(hi, lo, mask, seq):
                if not (isinstance(seq, int) and seq == 0):
                    pe.wait_ge(k_ready, seq)
                for n in range(2):
                    cols = slice(n * HALF, (n + 1) * HALF)
                    pe.matmul(ps_k[:, cols], masks[:, mask, :], bias[:, 1, cols], start=True, stop=False)
                    for c in range(CK):
                        mm = three_passes(ps_k[:, cols], hi[:, c, :], lo[:, c, :],
                                          wk_hi[:, c, cols], wk_lo[:, c, cols], c == CK - 1)
                    mm.then_inc(k_half_done, 1)

            def queries_of(t, slot):
                if not (isinstance(t, int) and t == 0):
                    pe.wait_ge(q_used, t)
                for n in range(2):
                    cols = slice(n * HALF, (n + 1) * HALF)
                    pe.matmul(ps_q[:, cols], masks[:, 0, :], bias[:, 0, cols], start=True, stop=False)
                    for c in range(CK):
                        mm = three_passes(ps_q[:, cols], xT_hi[:, slot, c, :], xT_lo[:, slot, c, :],
                                          wq_hi[:, c, cols], wq_lo[:, c, cols], c == CK - 1)
                mm.then_inc(q_done, 1)

            def turn(n):
                pe.wait_ge(att_ready, n + 1)
                if not (isinstance(n, int) and n == 0):
                    pe.wait_ge(attT_ready, n)
                for c in range(HK):
                    mm = pe.transpose(ps_t[:, c, :], att[:, c * P:(c + 1) * P], ident[:])
                mm.then_inc(attT_done, 1)

            def output_of(n):
                pe.wait_ge(attT_ready, n + 1)
                if not (isinstance(n, int) and n == 0):
                    pe.wait_ge(out_ready, n)
                for c in range(HK):
                    for p, (lhs, rhs) in enumerate(((attT_hi, wo_hi), (attT_hi, wo_lo), (attT_lo, wo_hi))):
                        mm = pe.matmul(ps_o[:], lhs[:, c, :], rhs[:, c, :], start=(c == 0 and p == 0),
                                       stop=(c == HK - 1 and p == 2))
                mm.then_inc(o_done, 1)

            pe.wait_ge(masks_ready, 1)
            pe.wait_ge(bias_ready, 1)
            pe.wait_ge(w_lo_ready, CK)
            pe.wait_ge(x_ready, 1)
            keys_of(xT_hi[:, 0], xT_lo[:, 0], 1, 0)
            pe.wait_ge(x_ready, 2)
            keys_of(xT_hi[:, 1], xT_lo[:, 1], 0, 1)
            pe.wait_ge(cond_ready, 1)
            keys_of(cond_hi, cond_lo, 0, 2)

            def values_of_aux():
                pe.wait_ge(wv_in, 16)
                pe.wait_ge(late_in, 16 * 3)
                for n in range(2):
                    cols = slice(n * HALF, (n + 1) * HALF)
                    dst = ps_t.rearrange("p c n -> p (c n)")[:, cols]
                    pe.matmul(dst, ones_row, bv_row[:, cols], start=True, stop=False)
                    for c in range(CK):
                        mm = pe.matmul(dst, cond_raw[:, c, :], products[:, c, cols], start=False, stop=(c == CK - 1))
                mm.then_inc(av_done, 1)

            def step(i, r):
                t, static = i * SLOTS + r, isinstance(i, int)
                if not (static and t >= TILES):
                    pe.wait_ge(x_ready, t + 3)
                    slot = (r + 2) % SLOTS
                    keys_of(xT_hi[:, slot], xT_lo[:, slot], 2 if static and t == TILES - 1 else 0, t + 3)
                if static and t == 0:
                    values_of_aux()
                    pe.wait_ge(w_lo_ready, 2 * CK)
                if not (static and t < 2):
                    turn(t - 2)
                if not (static and t >= TILES):
                    queries_of(t, (r + 1) % SLOTS)
                if static and t == 2:
                    pe.wait_ge(wo_lo_ready, CK)
                if not (static and t < 2):
                    output_of(t - 2)

            pipeline(pe, step, TILES + 1)

        @block.scalar
        def _(act):
            def copy(dst, src):
                return act.activation(dst, src, ACT.Copy)

            def x_high(u, slot, count):
                act.wait_ge(xT_in[slot % 2], 16 * count)
                copy(xT_hi[:, slot], xT_raw[:, slot % 2]).then_inc(x_hi_ready, 1)

            def keys_out(dst, seq):
                for n in range(2):
                    cols = slice(n * HALF, (n + 1) * HALF)
                    act.wait_ge(k_half_done, 2 * seq + n + 1)
                    ins = copy(dst[:, cols], ps_k[:, cols])
                ins.then_inc(k_ready, 1)

            x_high(0, 0, 1)
            for c in range(CK):
                act.wait_ge(wk_in[c], 16)
                copy(wk_hi[:, c, :], products[:, c, :]).then_inc(w_hi_ready, 1)
            act.wait_ge(small_in, 32)
            copy(masks[:], masks_raw).then_inc(masks_ready, 1)
            copy(bqk_high.bitcast(F32R), bqk_raw).then_inc(bias_hi_ready, 1)
            x_high(1, 1, 1)
            act.wait_ge(cond_in, 16)
            copy(cond_hi, cond_raw[:]).then_inc(cond_hi_ready, 1)

            def wq_high(c):
                act.wait_ge(wq_in[c], 16)
                copy(wq_hi[:, c, :], weighted[:, c, :]).then_inc(w_hi_ready, 1)

            act.wait_ge(bias_ready, 1)
            keys_out(keys[:, 0], 0)
            wq_high(0)
            wq_high(1)
            x_high(2, 2, 2)
            keys_out(keys[:, 1], 1)
            wq_high(2)
            wq_high(3)
            keys_out(aux_key, 2)

            def exp_of(t):
                act.wait_ge(shifted_ready, t + 1)
                act.activation(expd[:], shifted[:], ACT.Exp, scale=SCALE).then_inc(exp_ready, 1)

            def step(i, r):
                t, static = i * SLOTS + r, isinstance(i, int)
                if not (static and not 1 <= t <= TILES):
                    exp_of(t - 1)
                if not (static and t >= TILES):
                    if not (static and t < 2):
                        act.wait_ge(weighted_ready, 3 * (t - 1))
                    keys_out(keys[:, (r + 2) % SLOTS], t + 3)
                if static and t == 0:
                    for c in range(CK):
                        act.wait_ge(wo_in[c], 16)
                        copy(wo_hi[:, 2 * c:2 * c + 2, :], weighted[:, c, :].rearrange("p (c n) -> p c n", c=2)).then_inc(w_hi_ready, 1)
                    act.wait_ge(av_done, 1)
                    copy(aux_value[:], ps_t.rearrange("p c n -> p (c n)")).then_inc(av_ready, 1)
                if not (static and t < 2):
                    act.wait_ge(attT_done, t - 1)
                    if not (static and t < 3):
                        act.wait_ge(o_done, t - 2)
                    copy(attT_hi[:], ps_t[:]).then_inc(attT_hi_ready, 1)
                if not (static and t + 3 > TILES + 1):
                    if static and t == 0:
                        act.wait_ge(k_half_done, 6)
                    if static and t == 1:
                        act.wait_ge(k_half_done, 2)
                    if not (static and t < 2):
                        act.wait_ge(q_done, t - 1)
                    x_high(t + 3, (r + 3) % SLOTS, 2 * i + (r + 3) // 2 + 1)

            pipeline(act, step, TILES + 1)

        @block.vector
        def _(dve):
            dve.memset(low_row[:], -1.0).then_inc(rows_set, 1)
            dve.wait_ge(rows_set, 1)
            dve.memset(low_row[0:1, :], 0.0).then_inc(rows_set, 1)

            def low(dst, raw, hi):
                return dve.tensor_tensor(dst, raw, hi.bitcast(F32), ALU.subtract)

            for c in range(CK):
                dve.wait_ge(w_hi_ready, c + 1)
                low(wk_lo[:, c, :], products[:, c, :], wk_hi[:, c, :]).then_inc(w_lo_ready, 1)
            dve.wait_ge(bias_hi_ready, 1)
            dve.wait_ge(rows_set, 2)
            dve.scalar_tensor_tensor(bias[:], bqk_high, low_row[:, 0:1], bqk_raw,
                                     ALU.mult, ALU.add).then_inc(bias_ready, 1)
            for c in range(CK):
                dve.wait_ge(w_hi_ready, CK + c + 1)
                low(wq_lo[:, c, :], weighted[:, c, :], wq_hi[:, c, :]).then_inc(w_lo_ready, 1)

            def scores_of(t, r):
                dve.wait_ge(q_done, t + 1)
                dve.wait_ge(k_ready, t + 4)
                for j in range(TAPS):
                    k = aux_key[:] if j == AUX else keys[:, (r + j) % SLOTS, :]
                    ins = dve.tensor_tensor(products[:, j, :], ps_q[:], k, ALU.mult)
                ins.then_inc(q_used, 1)
                dve.wait_ge(q_used, t + 1)
                dve.tensor_reduce(scores[:], products.rearrange("p j (h d) -> p (j h) d", h=HEADS), AX.X,
                                  ALU.add).then_inc(scores_ready, 1)
                dve.wait_ge(scores_ready, t + 1)
                dve.tensor_reduce(peak[:], scores.rearrange("p j h -> p h j"), AX.X, ALU.max).then_inc(peak_ready, 1)
                dve.wait_ge(peak_ready, t + 1)
                dve.tensor_tensor(shifted[:], scores[:], peak[:].unsqueeze(1).to_broadcast([P, TAPS, HEADS]),
                                  ALU.subtract).then_inc(shifted_ready, 1)

            def weigh(t, r):
                dve.wait_ge(exp_ready, t + 1)
                dve.tensor_reduce(total[:], expd.rearrange("p j h -> p h j"), AX.X, ALU.add).then_inc(total_ready, 1)
                dve.wait_ge(total_ready, t + 1)
                dve.reciprocal(inverse[:], total[:]).then_inc(inverse_ready, 1)
                dve.wait_ge(inverse_ready, t + 1)
                if not (isinstance(t, int) and t == 0):
                    dve.wait_ge(aux_weighted, t)
                dve.tensor_tensor(alpha[:], expd[:], inverse[:].unsqueeze(1).to_broadcast([P, TAPS, HEADS]),
                                  ALU.mult).then_inc(alpha_ready, 1)
                dve.wait_ge(alpha_ready, t + 1)
                if not (isinstance(t, int) and t == 0):
                    dve.wait_ge(att_ready, t)
                for j in range(AUX):
                    dve.tensor_tensor(by_head(weighted[:, j, :]), by_head(keys[:, (r + j) % SLOTS, :]),
                                      bcast_heads(alpha[:, j, :]), ALU.mult).then_inc(weighted_ready, 1)

            def low_attT(n):
                dve.wait_ge(attT_hi_ready, n + 1)
                if not (isinstance(n, int) and n == 0):
                    dve.wait_ge(o_done, n)
                dve.tensor_tensor(attT_lo[:], ps_t[:], attT_hi[:].bitcast(F32), ALU.subtract).then_inc(attT_ready, 1)

            def add_residual(n, slot, sent, first):
                dve.wait_ge(o_done, n + 1)
                dve.wait_ge(resid_ready, n + 1)
                if not first:
                    dve.wait_ge(stored[slot], sent)
                dve.tensor_tensor(out_sb[:, slot, :], ps_o[:], resid[:, slot, :], ALU.add).then_inc(out_ready, 1)

            def step(i, r):
                t, static = i * SLOTS + r, isinstance(i, int)
                if static and t == 0:
                    dve.wait_ge(av_done, 1)
                if not (static and t >= TILES):
                    scores_of(t, r)
                if static and t == 0:
                    dve.wait_ge(w_hi_ready, 3 * CK)
                    dve.wait_ge(wo_lo_ready, CK)
                if not (static and not 2 <= t <= TILES + 1):
                    add_residual(t - 2, r % 2, 16 * (2 * i + r // 2 - 1), static and t < 4)
                if not (static and t >= TILES):
                    weigh(t, r)
                if not (static and not 1 <= t <= TILES):
                    low_attT(t - 1)

            pipeline(dve, step, TILES + 1)

        @block.gpsimd
        def _(pool):
            def low(dst, raw, hi):
                return pool.tensor_tensor(dst, raw, hi.bitcast(F32), ALU.subtract)

            def x_low(u, slot):
                pool.wait_ge(x_hi_ready, u + 1)
                low(xT_lo[:, slot], xT_raw[:, slot % 2], xT_hi[:, slot]).then_inc(x_ready, 1)

            x_low(0, 0)
            x_low(1, 1)
            pool.wait_ge(cond_hi_ready, 1)
            low(cond_lo, cond_raw[:], cond_hi).then_inc(cond_ready, 1)
            x_low(2, 2)

            def step(i, r):
                t, static = i * SLOTS + r, isinstance(i, int)
                if not (static and t + 3 > TILES + 1):
                    x_low(t + 3, (r + 3) % SLOTS)
                if not (static and not 2 <= t <= TILES + 1):
                    slot = r % 2
                    pool.wait_ge(resid_in[slot], 16 * (2 * i + r // 2))
                    pool.tensor_tensor(resid[:, slot, :], resid[:, slot, :], bo_rows[:], ALU.add).then_inc(resid_ready, 1)
                if static and t == 0:
                    for c in range(CK):
                        pool.wait_ge(w_hi_ready, 2 * CK + c + 1)
                        low(wo_lo[:, 2 * c:2 * c + 2, :], weighted[:, c, :].rearrange("p (c n) -> p c n", c=2),
                            wo_hi[:, 2 * c:2 * c + 2, :]).then_inc(wo_lo_ready, 1)
                    pool.wait_ge(av_ready, 1)
                    pool.wait_ge(wo_lo_ready, CK)
                if not (static and t >= TILES):
                    pool.wait_ge(alpha_ready, t + 1)
                    if not (static and t == 0):
                        pool.wait_ge(att_ready, t)
                    pool.tensor_tensor(by_head(weighted[:, AUX, :]), by_head(aux_value[:]),
                                       bcast_heads(alpha[:, AUX, :]), ALU.mult).then_inc(aux_weighted, 1)
                    pool.wait_ge(weighted_ready, 3 * t + 2)
                    pool.tensor_tensor(weighted[:, 0, :], weighted[:, 0, :], weighted[:, 1, :],
                                       ALU.add).then_inc(pair_summed, 1)
                    pool.wait_ge(weighted_ready, 3 * t + 3)
                    pool.wait_ge(aux_weighted, t + 1)
                    pool.tensor_tensor(weighted[:, 2, :], weighted[:, 2, :], weighted[:, AUX, :],
                                       ALU.add).then_inc(pair_summed, 1)
                    pool.wait_ge(pair_summed, 2 * t + 2)
                    if not (static and t == 0):
                        pool.wait_ge(attT_done, t)
                    pool.tensor_tensor(att[:], weighted[:, 0, :], weighted[:, 2, :],
                                       ALU.add).then_inc(att_ready, 1)

            pool.wait_ge(late_in, 16 * 3)
            pipeline(pool, step, TILES + 1)


def kernel(**inputs):
    import numpy as np
    import concourse.bacc as bacc
    from concourse import mybir as mb
    from concourse.bass_utils import run_bass_kernel_spmd as run

    x = np.asarray(inputs["x"])
    batches, length, _ = x.shape
    runs = P // batches
    padded = np.pad(x, ((0, 0), (1, 1), (0, 0)))
    tiles = [padded[:, u:u + length:TILES, :][:, :runs].reshape(P, CK, P).transpose(2, 1, 0) for u in range(TILES + 2)]
    cond = np.repeat(np.asarray(inputs["cond_1024"]), runs, axis=0).reshape(P, CK, P).transpose(2, 1, 0)

    def weight(name, chunks):
        w = np.asarray(inputs[name])
        return w.reshape(chunks, P, w.shape[1]).transpose(1, 0, 2)

    def row(name):
        return np.asarray(inputs[name]).reshape(1, -1)

    masks = np.ones((2, 3, P), np.float32)
    masks[:, 1, 0::runs] = 0.0
    masks[:, 2, runs - 1::runs] = 0.0
    bqk = np.stack([row("L0_cond_WQ_b")[0], row("L0_cond_WK_b")[0]])
    arrays = {
        "xT": np.stack(tiles),
        "x_tokens": x.reshape(P, TILES, C),
        "condT": cond,
        "wq": weight("L0_cond_WQ_w", CK),
        "wk": weight("L0_cond_WK_w", CK),
        "wv": weight("L0_cond_WV_w", CK),
        "wo": weight("L0_cond_WO_w", HK).reshape(P, CK, CH),
        "bqk": np.stack([bqk, bqk]),
        "bv": row("L0_cond_WV_b"),
        "bo": np.broadcast_to(row("L0_cond_WO_b"), (P, C)),
        "ident": np.eye(P, dtype=np.float32),
        "masks": masks,
    }
    arrays = {k: np.ascontiguousarray(v) for k, v in arrays.items()}
    nc = bacc.Bacc("TRN2", target_bir_lowering=False, num_devices=1)
    args = [nc.dram_tensor("in_" + k, v.shape, mb.dt.from_np(v.dtype), kind="ExternalInput").ap() for k, v in arrays.items()]
    xT, x_ap, condT, wq, wk, wv, wo, bqk_ap, bv, bo, ident, masks_ap = args
    out = nc.dram_tensor("out", (P, TILES, C), mb.dt.float32, kind="ExternalOutput").ap()
    build(nc, xT, x_ap, condT, wq, wk, wv, wo, bqk_ap, bv, bo, ident, masks_ap, out)
    got = run(nc, [{"in_" + k: v for k, v in arrays.items()}], core_ids=[0])
    return got.results[0]["out"].reshape(batches, length, C)
```

```python
from contextlib import ExitStack

import concourse.bass as bass
from concourse import mybir

F32 = mybir.dt.float32
F32R = mybir.dt.float32r
ALU = mybir.AluOpType
ACT = mybir.ActivationFunctionType
AX = mybir.AxisListType

P = 128
C = 512
HEADS = 16
HD = 64
CH = HEADS * HD
CK = C // P
HK = CH // P
HALF = 512
TILES = 32
SLOTS = 4
SCALE = HD ** -0.5
TAPS = 4
AUX = TAPS - 1


def build(nc, xT, x, condT, wq, wk, wv, wo, bq, bk, bv, bo, ident_in, masks_in, out):
    with ExitStack() as ctx:
        def sb(name, shape, dt=F32):
            return ctx.enter_context(nc.sbuf_tensor(name, shape, dt))

        def ps(name, shape):
            return ctx.enter_context(nc.psum_tensor(name, shape, F32))

        def sem(name):
            return ctx.enter_context(nc.semaphore(name))

        wk_hi, wk_lo = sb("wk_hi", [P, CK, CH], F32R), sb("wk_lo", [P, CK, CH], F32R)
        wq_hi, wq_lo = sb("wq_hi", [P, CK, CH], F32R), sb("wq_lo", [P, CK, CH], F32R)
        wo_hi, wo_lo = sb("wo_hi", [P, HK, C], F32R), sb("wo_lo", [P, HK, C], F32R)
        products = sb("products", [P, TAPS, CH])
        weighted = sb("weighted", [P, TAPS, CH])
        keys = sb("keys", [P, SLOTS, CH])
        aux_key = sb("aux_key", [P, CH])
        aux_value = sb("aux_value", [P, CH])
        att = sb("att", [P, CH])
        attT_hi, attT_lo = sb("attT_hi", [P, HK, P], F32R), sb("attT_lo", [P, HK, P], F32R)
        xT_raw = sb("xT_raw", [P, 2, CK, P])
        xT_hi, xT_lo = sb("xT_hi", [P, SLOTS, CK, P], F32R), sb("xT_lo", [P, SLOTS, CK, P], F32R)
        cond_raw = sb("cond_raw", [P, CK, P])
        resid = sb("resid", [P, 2, C])
        bq_rows, bk_rows = sb("bq_rows", [P, CH]), sb("bk_rows", [P, CH])
        bo_rows = sb("bo_rows", [P, C])
        ident = sb("ident", [P, P])
        masks = sb("masks", [2, 3, P], F32R)
        low_row = sb("low_row", [2, 1])
        bk_parts = sb("bk_parts", [2, CH], F32R)
        scores = sb("scores", [P, TAPS, HEADS])
        peak = sb("peak", [P, HEADS])
        shifted = sb("shifted", [P, TAPS, HEADS])
        expd = sb("expd", [P, TAPS, HEADS])
        total = sb("total", [P, HEADS])
        inverse = sb("inverse", [P, HEADS])
        alpha = sb("alpha", [P, TAPS, HEADS])
        bk_high = keys[0:2, 0, :]
        bv_row = att[0:1, :]
        masks_raw = aux_value[0:2, 0:3 * P].rearrange("q (m n) -> q m n", m=3)
        ones_row = masks_raw[0:1, 0, :]
        cond_hi, cond_lo = xT_hi[:, 3], xT_lo[:, 3]

        ps_k = ps("ps_k", [P, CH])
        ps_q = ps("ps_q", [P, CH])
        ps_t = ps("ps_t", [P, HK, P])
        ps_o = ps("ps_o", [P, C])

        wk_in = [sem(f"wk_in{c}") for c in range(CK)]
        wq_in = [sem(f"wq_in{c}") for c in range(CK)]
        wv_in = sem("wv_in")
        wo_in = [sem(f"wo_in{c}") for c in range(CK)]
        bk_in = sem("bk_in")
        masks_in_sem = sem("masks_in")
        bq_in = sem("bq_in")
        late_in = sem("late_in")
        cond_in = sem("cond_in")
        xT_in = [sem(f"xT_in{s}") for s in range(2)]
        resid_in = [sem(f"resid_in{s}") for s in range(2)]
        stored = [sem(f"stored{s}") for s in range(2)]
        w_hi_ready = sem("w_hi_ready")
        w_lo_ready = sem("w_lo_ready")
        wo_lo_ready = sem("wo_lo_ready")
        bias_hi_ready = sem("bias_hi_ready")
        masks_ready = sem("masks_ready")
        bias_ready = sem("bias_ready")
        rows_set = sem("rows_set")
        cond_hi_ready = sem("cond_hi_ready")
        cond_ready = sem("cond_ready")
        x_hi_ready = sem("x_hi_ready")
        x_ready = sem("x_ready")
        k_half_done = sem("k_half_done")
        k_copied = sem("k_copied")
        k_ready = sem("k_ready")
        q_biased = sem("q_biased")
        av_done = sem("av_done")
        av_ready = sem("av_ready")
        q_done = sem("q_done")
        q_used = sem("q_used")
        scores_ready = sem("scores_ready")
        peak_ready = sem("peak_ready")
        shifted_ready = sem("shifted_ready")
        exp_ready = sem("exp_ready")
        total_ready = sem("total_ready")
        inverse_ready = sem("inverse_ready")
        alpha_ready = sem("alpha_ready")
        own_weighted = sem("own_weighted")
        next_weighted = sem("next_weighted")
        aux_weighted = sem("aux_weighted")
        pair_summed = sem("pair_summed")
        att_ready = sem("att_ready")
        attT_done = sem("attT_done")
        attT_hi_ready = sem("attT_hi_ready")
        attT_ready = sem("attT_ready")
        resid_ready = sem("resid_ready")
        o_done = sem("o_done")
        out_ready = sem("out_ready")

        block = ctx.enter_context(nc.Block())

        def pipeline(eng, step, last):
            for t in range(SLOTS):
                step(0, t)
            with eng.Fori(1, TILES // SLOTS - 1) as i:
                for r in range(SLOTS):
                    step(i, r)
            for t in range(TILES - SLOTS, last + 1):
                step(*divmod(t, SLOTS))

        def bcast_heads(row):
            return row.unsqueeze(2).to_broadcast([P, HEADS, HD])

        def by_head(row):
            return row.rearrange("p (h d) -> p h d", h=HEADS)

        @block.sync
        def _(sp):
            def load_x(u, slot):
                sp.dma_start(xT_raw[:, slot], xT[u]).then_inc(xT_in[slot], 16)

            sp.dma_start(xT_raw[:, 0], xT[0]).then_inc(xT_in[0], 16)
            for c in range(CK):
                sp.dma_start(products[:, c, :], wk[:, c, :]).then_inc(wk_in[c], 16)
            sp.dma_start(bk_rows[:], bk).then_inc(bk_in, 16)
            sp.dma_start(masks_raw, masks_in).then_inc(masks_in_sem, 16)
            load_x(1, 1)
            for c in range(CK):
                sp.dma_start(weighted[:, c, :], wq[:, c, :]).then_inc(wq_in[c], 16)
            sp.dma_start(bq_rows[:], bq).then_inc(bq_in, 16)
            sp.dma_start(cond_raw[:], condT).then_inc(cond_in, 16)
            sp.wait_ge(x_ready, 1)
            load_x(2, 0)
            sp.dma_start(bv_row, bv).then_inc(late_in, 16)
            sp.dma_start(bo_rows[:], bo).then_inc(late_in, 16)
            sp.dma_start(ident[:], ident_in).then_inc(late_in, 16)
            sp.wait_ge(w_hi_ready, CK)
            sp.wait_ge(w_lo_ready, CK)
            sp.dma_start(products[:], wv).then_inc(wv_in, 16)
            sp.wait_ge(x_ready, 2)
            load_x(3, 1)
            sp.wait_ge(w_hi_ready, 2 * CK)
            sp.wait_ge(w_lo_ready, 2 * CK)
            for c in range(CK):
                sp.dma_start(weighted[:, c, :], wo[:, c, :]).then_inc(wo_in[c], 16)

            def step(i, r):
                t, static = i * SLOTS + r, isinstance(i, int)
                if not (static and t + 4 > TILES + 1):
                    sp.wait_ge(x_ready, t + 3)
                    load_x(t + 4, r % 2)
                slot = (r + 1) % 2
                if not (static and t < 3):
                    sp.wait_ge(out_ready, t - 2)
                    sp.dma_start(out[:, t - 3, :], resid[:, slot, :]).then_inc(stored[slot], 16)
                if not (static and not 1 <= t <= TILES):
                    if not (static and t < 3):
                        sp.wait_ge(stored[slot], 16 * (2 * i + (r - 1) // 2))
                    sp.dma_start(resid[:, slot, :], x[:, t - 1, :]).then_inc(resid_in[slot], 16)

            pipeline(sp, step, TILES + 2)
            for s in range(2):
                sp.wait_ge(stored[s], 16 * (TILES // 2))

        @block.tensor
        def _(pe):
            def three_passes(dst, hi, lo, w_hi, w_lo, first, last):
                pe.matmul(dst, hi, w_hi, start=first, stop=False)
                pe.matmul(dst, hi, w_lo, start=False, stop=False)
                return pe.matmul(dst, lo, w_hi, start=False, stop=last)

            def keys_of(hi, lo, mask, seq):
                if not (isinstance(seq, int) and seq == 0):
                    pe.wait_ge(k_copied, seq)
                for n in range(2):
                    cols = slice(n * HALF, (n + 1) * HALF)
                    if mask is not None:
                        pe.matmul(ps_k[:, cols], masks[:, mask, :], bk_parts[:, cols], start=True, stop=False)
                    for c in range(CK):
                        mm = three_passes(ps_k[:, cols], hi[:, c, :], lo[:, c, :],
                                          wk_hi[:, c, cols], wk_lo[:, c, cols],
                                          mask is None and c == 0, c == CK - 1)
                    mm.then_inc(k_half_done, 1)

            def queries_of(t, slot):
                if not (isinstance(t, int) and t == 0):
                    pe.wait_ge(q_used, t)
                for n in range(2):
                    cols = slice(n * HALF, (n + 1) * HALF)
                    for c in range(CK):
                        mm = three_passes(ps_q[:, cols], xT_hi[:, slot, c, :], xT_lo[:, slot, c, :],
                                          wq_hi[:, c, cols], wq_lo[:, c, cols], c == 0, c == CK - 1)
                mm.then_inc(q_done, 1)

            def turn(n):
                pe.wait_ge(att_ready, n + 1)
                if not (isinstance(n, int) and n == 0):
                    pe.wait_ge(attT_ready, n)
                for c in range(HK):
                    mm = pe.transpose(ps_t[:, c, :], att[:, c * P:(c + 1) * P], ident[:])
                mm.then_inc(attT_done, 1)

            def output_of(n):
                pe.wait_ge(attT_ready, n + 1)
                if not (isinstance(n, int) and n == 0):
                    pe.wait_ge(out_ready, n)
                for c in range(HK):
                    mm = three_passes(ps_o[:], attT_hi[:, c, :], attT_lo[:, c, :],
                                      wo_hi[:, c, :], wo_lo[:, c, :], c == 0, c == HK - 1)
                mm.then_inc(o_done, 1)

            pe.wait_ge(masks_ready, 1)
            pe.wait_ge(bias_ready, 1)
            pe.wait_ge(w_lo_ready, CK)
            pe.wait_ge(x_ready, 1)
            keys_of(xT_hi[:, 0], xT_lo[:, 0], 1, 0)
            pe.wait_ge(x_ready, 2)
            keys_of(xT_hi[:, 1], xT_lo[:, 1], 0, 1)

            def values_of_aux():
                pe.wait_ge(wv_in, 16)
                pe.wait_ge(late_in, 16 * 3)
                for n in range(2):
                    cols = slice(n * HALF, (n + 1) * HALF)
                    dst = ps_t.rearrange("p c n -> p (c n)")[:, cols]
                    pe.matmul(dst, ones_row, bv_row[:, cols], start=True, stop=False)
                    for c in range(CK):
                        mm = pe.matmul(dst, cond_raw[:, c, :], products[:, c, cols], start=False, stop=(c == CK - 1))
                mm.then_inc(av_done, 1)

            def step(i, r):
                t, static = i * SLOTS + r, isinstance(i, int)
                if not (static and t >= TILES):
                    pe.wait_ge(x_ready, t + 3)
                    slot = (r + 2) % SLOTS
                    if static and t == 0:
                        keys_of(xT_hi[:, slot], xT_lo[:, slot], 0, 2)
                        pe.wait_ge(w_lo_ready, 2 * CK)
                    else:
                        keys_of(xT_hi[:, slot], xT_lo[:, slot], 2 if static and t == TILES - 1 else None, t + 3)
                if not (static and t < 2):
                    turn(t - 2)
                if not (static and t >= TILES):
                    queries_of(t, (r + 1) % SLOTS)
                if static and t == 0:
                    pe.wait_ge(cond_ready, 1)
                    keys_of(cond_hi, cond_lo, 0, 3)
                    values_of_aux()
                if static and t == 2:
                    pe.wait_ge(wo_lo_ready, CK)
                if not (static and t < 2):
                    output_of(t - 2)

            pipeline(pe, step, TILES + 1)

        @block.scalar
        def _(act):
            def copy(dst, src):
                return act.activation(dst, src, ACT.Copy)

            def x_high(u, slot, count):
                act.wait_ge(xT_in[slot % 2], 16 * count)
                copy(xT_hi[:, slot], xT_raw[:, slot % 2]).then_inc(x_hi_ready, 1)

            def keys_out(dst, seq):
                for n in range(2):
                    cols = slice(n * HALF, (n + 1) * HALF)
                    act.wait_ge(k_half_done, 2 * seq + n + 1)
                    ins = copy(dst[:, cols], ps_k[:, cols])
                ins.then_inc(k_copied, 1)

            x_high(0, 0, 1)
            for c in range(CK):
                act.wait_ge(wk_in[c], 16)
                copy(wk_hi[:, c, :], products[:, c, :]).then_inc(w_hi_ready, 1)
            act.wait_ge(masks_in_sem, 16)
            copy(masks[:], masks_raw).then_inc(masks_ready, 1)
            act.wait_ge(bk_in, 16)
            copy(bk_high.bitcast(F32R), bk_rows[0:2, :]).then_inc(bias_hi_ready, 1)
            x_high(1, 1, 1)

            def wq_high(c):
                act.wait_ge(wq_in[c], 16)
                copy(wq_hi[:, c, :], weighted[:, c, :]).then_inc(w_hi_ready, 1)

            wq_high(0)
            wq_high(1)
            act.wait_ge(bias_ready, 1)
            keys_out(keys[:, 0], 0)
            wq_high(2)
            x_high(2, 2, 2)
            wq_high(3)
            keys_out(keys[:, 1], 1)
            act.wait_ge(cond_in, 16)
            copy(cond_hi, cond_raw[:]).then_inc(cond_hi_ready, 1)

            def weigh_two(t, r):
                act.wait_ge(alpha_ready, t + 1)
                if not (isinstance(t, int) and t == 0):
                    act.wait_ge(att_ready, t)
                for j in (1, 2):
                    for h in range(HEADS):
                        cols = slice(h * HD, (h + 1) * HD)
                        ins = act.activation(weighted[:, j, cols], keys[:, (r + j) % SLOTS, cols], ACT.Copy,
                                             scale=alpha[:, j, h:h + 1])
                    ins.then_inc(next_weighted, 1)

            def exp_of(t):
                act.wait_ge(shifted_ready, t + 1)
                act.activation(expd[:], shifted[:], ACT.Exp, scale=SCALE).then_inc(exp_ready, 1)

            def step(i, r):
                t, static = i * SLOTS + r, isinstance(i, int)
                if not (static and not 1 <= t <= TILES):
                    exp_of(t - 1)
                if not (static and t >= TILES):
                    if not (static and t < 2):
                        act.wait_ge(own_weighted, t - 1)
                    if static and t == 0:
                        keys_out(keys[:, 2], 2)
                        keys_out(aux_key, 3)
                    else:
                        keys_out(keys[:, (r + 2) % SLOTS], t + 3)
                if static and t == 0:
                    for c in range(CK):
                        act.wait_ge(wo_in[c], 16)
                        copy(wo_hi[:, 2 * c:2 * c + 2, :],
                             weighted[:, c, :].rearrange("p (c n) -> p c n", c=2)).then_inc(w_hi_ready, 1)
                if not (static and t < 2):
                    act.wait_ge(attT_done, t - 1)
                    if not (static and t < 3):
                        act.wait_ge(o_done, t - 2)
                    copy(attT_hi[:], ps_t[:]).then_inc(attT_hi_ready, 1)
                if not (static and t + 3 > TILES + 1):
                    if static and t == 1:
                        act.wait_ge(k_half_done, 2)
                    if not (static and t < 2):
                        act.wait_ge(q_done, t - 1)
                    x_high(t + 3, (r + 3) % SLOTS, 2 * i + (r + 3) // 2 + 1)
                if static and t == 0:
                    act.wait_ge(av_done, 1)
                    copy(aux_value[:], ps_t.rearrange("p c n -> p (c n)")).then_inc(av_ready, 1)
                if not (static and not 1 <= t <= TILES):
                    if static and t == 1:
                        act.wait_ge(wo_lo_ready, CK)
                    weigh_two(t - 1, (r - 1) % SLOTS)

            pipeline(act, step, TILES + 1)

        @block.vector
        def _(dve):
            dve.memset(low_row[:], -1.0).then_inc(rows_set, 1)
            dve.wait_ge(rows_set, 1)
            dve.memset(low_row[0:1, :], 0.0).then_inc(rows_set, 1)

            def low(dst, raw, hi):
                return dve.tensor_tensor(dst, raw, hi.bitcast(F32), ALU.subtract)

            def x_low(u, slot):
                dve.wait_ge(x_hi_ready, u + 1)
                low(xT_lo[:, slot], xT_raw[:, slot % 2], xT_hi[:, slot]).then_inc(x_ready, 1)

            x_low(0, 0)
            for c in range(CK):
                dve.wait_ge(w_hi_ready, c + 1)
                low(wk_lo[:, c, :], products[:, c, :], wk_hi[:, c, :]).then_inc(w_lo_ready, 1)
            dve.wait_ge(bias_hi_ready, 1)
            dve.wait_ge(rows_set, 2)
            dve.scalar_tensor_tensor(bk_parts[:], bk_high, low_row[:, 0:1], bk_rows[0:2, :],
                                     ALU.mult, ALU.add).then_inc(bias_ready, 1)
            x_low(1, 1)
            for c in range(CK):
                if c == 3:
                    x_low(2, 2)
                dve.wait_ge(w_hi_ready, CK + c + 1)
                low(wq_lo[:, c, :], weighted[:, c, :], wq_hi[:, c, :]).then_inc(w_lo_ready, 1)
            dve.wait_ge(cond_hi_ready, 1)
            low(cond_lo, cond_raw[:], cond_hi).then_inc(cond_ready, 1)

            def scores_of(t, r):
                dve.wait_ge(q_done, t + 1)
                if isinstance(t, int) and t == 0:
                    dve.wait_ge(bq_in, 16)
                    dve.wait_ge(av_done, 1)
                dve.tensor_tensor(ps_q[:], ps_q[:], bq_rows[:], ALU.add).then_inc(q_biased, 1)
                dve.wait_ge(q_biased, t + 1)
                if isinstance(t, int) and t == 0:
                    dve.wait_ge(k_copied, 4)
                elif isinstance(t, int) and t == TILES - 1:
                    dve.wait_ge(k_copied, t + 4)
                    dve.wait_ge(k_ready, t - 1)
                else:
                    dve.wait_ge(k_ready, t)
                for j in range(TAPS):
                    k = aux_key[:] if j == AUX else keys[:, (r + j) % SLOTS, :]
                    ins = dve.tensor_tensor(products[:, j, :], ps_q[:], k, ALU.mult)
                ins.then_inc(q_used, 1)
                dve.wait_ge(q_used, t + 1)
                dve.tensor_reduce(scores[:], products.rearrange("p j (h d) -> p (j h) d", h=HEADS), AX.X,
                                  ALU.add).then_inc(scores_ready, 1)
                dve.wait_ge(scores_ready, t + 1)
                dve.tensor_reduce(peak[:], scores.rearrange("p j h -> p h j"), AX.X, ALU.max).then_inc(peak_ready, 1)
                dve.wait_ge(peak_ready, t + 1)
                dve.tensor_tensor(shifted[:], scores[:], peak[:].unsqueeze(1).to_broadcast([P, TAPS, HEADS]),
                                  ALU.subtract).then_inc(shifted_ready, 1)

            def weigh(t, r):
                dve.wait_ge(exp_ready, t + 1)
                dve.tensor_reduce(total[:], expd.rearrange("p j h -> p h j"), AX.X, ALU.add).then_inc(total_ready, 1)
                dve.wait_ge(total_ready, t + 1)
                dve.reciprocal(inverse[:], total[:]).then_inc(inverse_ready, 1)
                dve.wait_ge(inverse_ready, t + 1)
                if not (isinstance(t, int) and t == 0):
                    dve.wait_ge(aux_weighted, t)
                    dve.wait_ge(next_weighted, 2 * t)
                dve.tensor_tensor(alpha[:], expd[:], inverse[:].unsqueeze(1).to_broadcast([P, TAPS, HEADS]),
                                  ALU.mult).then_inc(alpha_ready, 1)
                dve.wait_ge(alpha_ready, t + 1)
                if not (isinstance(t, int) and t == 0):
                    dve.wait_ge(att_ready, t)
                dve.tensor_tensor(by_head(weighted[:, 0, :]), by_head(keys[:, r, :]),
                                  bcast_heads(alpha[:, 0, :]), ALU.mult).then_inc(own_weighted, 1)

            def low_attT(n):
                dve.wait_ge(attT_hi_ready, n + 1)
                if not (isinstance(n, int) and n == 0):
                    dve.wait_ge(o_done, n)
                dve.tensor_tensor(attT_lo[:], ps_t[:], attT_hi[:].bitcast(F32), ALU.subtract).then_inc(attT_ready, 1)

            def add_residual(n, slot):
                dve.wait_ge(o_done, n + 1)
                dve.wait_ge(resid_ready, n + 1)
                dve.tensor_tensor(resid[:, slot, :], ps_o[:], resid[:, slot, :], ALU.add).then_inc(out_ready, 1)

            def step(i, r):
                t, static = i * SLOTS + r, isinstance(i, int)
                if not (static and (t == 0 or t + 3 > TILES + 1)):
                    x_low(t + 3, (r + 3) % SLOTS)
                if not (static and t >= TILES):
                    scores_of(t, r)
                if static and t == 0:
                    x_low(3, 3)
                    dve.wait_ge(w_hi_ready, 3 * CK)
                    dve.wait_ge(wo_lo_ready, CK)
                if not (static and not 2 <= t <= TILES + 1):
                    add_residual(t - 2, r % 2)
                if not (static and t >= TILES):
                    weigh(t, r)
                if not (static and not 1 <= t <= TILES):
                    low_attT(t - 1)

            pipeline(dve, step, TILES + 1)

        @block.gpsimd
        def _(pool):
            def low(dst, raw, hi):
                return pool.tensor_tensor(dst, raw, hi.bitcast(F32), ALU.subtract)

            def sum_values(t):
                first = isinstance(t, int) and t == 0
                pool.wait_ge(aux_weighted, t + 1)
                pool.wait_ge(own_weighted, t + 1)
                pool.tensor_tensor(weighted[:, 0, :], weighted[:, 0, :], weighted[:, AUX, :],
                                   ALU.add).then_inc(pair_summed, 1)
                pool.wait_ge(next_weighted, 2 * t + 2)
                pool.tensor_tensor(weighted[:, 1, :], weighted[:, 1, :], weighted[:, 2, :],
                                   ALU.add).then_inc(pair_summed, 1)
                pool.wait_ge(pair_summed, 2 * t + 2)
                if not first:
                    pool.wait_ge(attT_done, t)
                pool.tensor_tensor(att[:], weighted[:, 0, :], weighted[:, 1, :], ALU.add).then_inc(att_ready, 1)

            def step(i, r):
                t, static = i * SLOTS + r, isinstance(i, int)
                if static and t == 0:
                    for c in range(CK):
                        pool.wait_ge(w_hi_ready, 2 * CK + c + 1)
                        low(wo_lo[:, 2 * c:2 * c + 2, :], weighted[:, c, :].rearrange("p (c n) -> p c n", c=2),
                            wo_hi[:, 2 * c:2 * c + 2, :]).then_inc(wo_lo_ready, 1)
                    pool.wait_ge(av_ready, 1)
                    pool.wait_ge(wo_lo_ready, CK)
                if not (static and not 1 <= t <= TILES):
                    pool.wait_ge(alpha_ready, t)
                    if not (static and t == 1):
                        pool.wait_ge(att_ready, t - 1)
                    pool.tensor_tensor(by_head(weighted[:, AUX, :]), by_head(aux_value[:]),
                                       bcast_heads(alpha[:, AUX, :]), ALU.mult).then_inc(aux_weighted, 1)
                if not (static and not 1 <= t < TILES):
                    pool.wait_ge(k_copied, t + 4)
                    slot = (r + 2) % SLOTS
                    if not (static and t == TILES - 1):
                        pool.tensor_tensor(keys[:, slot, :], keys[:, slot, :], bk_rows[:], ALU.add).then_inc(k_ready, 1)
                if not (static and not 1 <= t <= TILES):
                    sum_values(t - 1)
                if not (static and not 2 <= t <= TILES + 1):
                    slot = r % 2
                    pool.wait_ge(resid_in[slot], 16 * (2 * i + r // 2))
                    pool.tensor_tensor(resid[:, slot, :], resid[:, slot, :], bo_rows[:], ALU.add).then_inc(resid_ready, 1)

            pool.wait_ge(late_in, 16 * 3)
            pipeline(pool, step, TILES + 1)


def kernel(**inputs):
    import numpy as np
    import concourse.bacc as bacc
    from concourse import mybir as mb
    from concourse.bass_utils import run_bass_kernel_spmd as run

    x = np.asarray(inputs["x"])
    batches, length, _ = x.shape
    runs = P // batches
    padded = np.pad(x, ((0, 0), (1, 1), (0, 0)))
    tiles = [padded[:, u:u + length:TILES, :][:, :runs].reshape(P, CK, P).transpose(2, 1, 0) for u in range(TILES + 2)]
    cond = np.repeat(np.asarray(inputs["cond_1024"]), runs, axis=0).reshape(P, CK, P).transpose(2, 1, 0)

    def weight(name, chunks):
        w = np.asarray(inputs[name])
        return w.reshape(chunks, P, w.shape[1]).transpose(1, 0, 2)

    def rows(name):
        b = np.asarray(inputs[name])
        return np.broadcast_to(b, (P, b.size))

    masks = np.ones((2, 3, P), np.float32)
    masks[:, 1, 0::runs] = 0.0
    masks[:, 2, runs - 1::runs] = 0.0
    arrays = {
        "xT": np.stack(tiles),
        "x_tokens": x.reshape(P, TILES, C),
        "condT": cond,
        "wq": weight("L0_cond_WQ_w", CK),
        "wk": weight("L0_cond_WK_w", CK),
        "wv": weight("L0_cond_WV_w", CK),
        "wo": weight("L0_cond_WO_w", HK).reshape(P, CK, CH),
        "bq": rows("L0_cond_WQ_b"),
        "bk": rows("L0_cond_WK_b"),
        "bv": np.asarray(inputs["L0_cond_WV_b"]).reshape(1, -1),
        "bo": rows("L0_cond_WO_b"),
        "ident": np.eye(P, dtype=np.float32),
        "masks": masks,
    }
    arrays = {k: np.ascontiguousarray(v) for k, v in arrays.items()}
    nc = bacc.Bacc("TRN2", target_bir_lowering=False, num_devices=1)
    args = [nc.dram_tensor("in_" + k, v.shape, mb.dt.from_np(v.dtype), kind="ExternalInput").ap() for k, v in arrays.items()]
    xT, x_ap, condT, wq, wk, wv, wo, bq, bk, bv, bo, ident, masks_ap = args
    out = nc.dram_tensor("out", (P, TILES, C), mb.dt.float32, kind="ExternalOutput").ap()
    build(nc, xT, x_ap, condT, wq, wk, wv, wo, bq, bk, bv, bo, ident, masks_ap, out)
    got = run(nc, [{"in_" + k: v for k, v in arrays.items()}], core_ids=[0])
    return got.results[0]["out"].reshape(batches, length, C)
```

```python
from contextlib import ExitStack

import concourse.bass as bass
from concourse import mybir

F32 = mybir.dt.float32
F32R = mybir.dt.float32r
ALU = mybir.AluOpType
ACT = mybir.ActivationFunctionType
AX = mybir.AxisListType

P = 128
C = 512
HEADS = 16
HD = 64
CH = HEADS * HD
CK = C // P
HK = CH // P
HALF = 512
TILES = 32
SLOTS = 4
SCALE = HD ** -0.5
BATCHES = 4
TAPS = 4
AUX = TAPS - 1


def build(nc, xT, x, condT, wq, wk, wv, wo, bq, bk, bv, bo, ident_in, masks_in, zeros_in, out):
    halo = nc.dram_tensor("halo", (P, CH), F32, kind="Internal").ap()
    with ExitStack() as ctx:
        def sb(name, shape, dt=F32):
            return ctx.enter_context(nc.sbuf_tensor(name, shape, dt))

        def ps(name, shape):
            return ctx.enter_context(nc.psum_tensor(name, shape, F32))

        def sem(name):
            return ctx.enter_context(nc.semaphore(name))

        wk_hi, wk_lo = sb("wk_hi", [P, CK, CH], F32R), sb("wk_lo", [P, CK, CH], F32R)
        wq_hi, wq_lo = sb("wq_hi", [P, CK, CH], F32R), sb("wq_lo", [P, CK, CH], F32R)
        wo_hi, wo_lo = sb("wo_hi", [P, HK, C], F32R), sb("wo_lo", [P, HK, C], F32R)
        products = sb("products", [P, TAPS, CH])
        weighted = sb("weighted", [P, TAPS, CH])
        keys = sb("keys", [P, SLOTS, CH])
        aux_key = sb("aux_key", [P, CH])
        aux_value = sb("aux_value", [P, CH])
        att = sb("att", [P, CH])
        attT_hi, attT_lo = sb("attT_hi", [P, HK, P], F32R), sb("attT_lo", [P, HK, P], F32R)
        xT_raw = sb("xT_raw", [P, 2, CK, P])
        xT_hi, xT_lo = sb("xT_hi", [P, SLOTS, CK, P], F32R), sb("xT_lo", [P, SLOTS, CK, P], F32R)
        cond_raw = sb("cond_raw", [P, CK, P])
        resid = sb("resid", [P, 2, C])
        bq_rows, bk_rows = sb("bq_rows", [P, CH]), sb("bk_rows", [P, CH])
        bo_rows = sb("bo_rows", [P, C])
        ident = sb("ident", [P, P])
        masks = sb("masks", [2, 2, P], F32R)
        low_row = sb("low_row", [2, 1])
        bk_parts = sb("bk_parts", [2, CH], F32R)
        scores = sb("scores", [P, TAPS, HEADS])
        peak = sb("peak", [P, HEADS])
        shifted = sb("shifted", [P, TAPS, HEADS])
        expd = sb("expd", [P, TAPS, HEADS])
        total = sb("total", [P, HEADS])
        inverse = sb("inverse", [P, HEADS])
        alpha = sb("alpha", [P, TAPS, HEADS])
        bk_high = keys[0:2, 3, :]
        bk_raw = keys[0:2, 2, :]
        bv_rows = att[:]
        masks_raw = aux_value[0:2, 0:2 * P].rearrange("q (m n) -> q m n", m=2)
        cond_hi, cond_lo = xT_hi[:, 3], xT_lo[:, 3]

        ps_k = ps("ps_k", [P, CH])
        ps_q = ps("ps_q", [P, CH])
        ps_t = ps("ps_t", [P, HK, P])
        ps_o = ps("ps_o", [P, C])

        wk_in = [sem(f"wk_in{c}") for c in range(CK)]
        wq_in = [sem(f"wq_in{c}") for c in range(CK)]
        wv_in = sem("wv_in")
        wo_in = [sem(f"wo_in{c}") for c in range(CK)]
        bk_in = sem("bk_in")
        small_in = sem("small_in")
        bq_in = sem("bq_in")
        bv_in = sem("bv_in")
        late_in = sem("late_in")
        cond_in = sem("cond_in")
        xT_in = [sem(f"xT_in{s}") for s in range(2)]
        resid_in = [sem(f"resid_in{s}") for s in range(2)]
        halo_saved = sem("halo_saved")
        halo_in = sem("halo_in")
        stored = [sem(f"stored{s}") for s in range(2)]
        w_hi_ready = sem("w_hi_ready")
        w_lo_ready = sem("w_lo_ready")
        bias_hi_ready = sem("bias_hi_ready")
        masks_ready = sem("masks_ready")
        bias_ready = sem("bias_ready")
        rows_set = sem("rows_set")
        cond_hi_ready = sem("cond_hi_ready")
        cond_ready = sem("cond_ready")
        x_hi_ready = sem("x_hi_ready")
        x_ready = sem("x_ready")
        k_half_done = sem("k_half_done")
        k_copied = sem("k_copied")
        k_ready = sem("k_ready")
        q_biased = sem("q_biased")
        av_done = sem("av_done")
        av_ready = sem("av_ready")
        q_done = sem("q_done")
        q_used = sem("q_used")
        scores_ready = sem("scores_ready")
        peak_ready = sem("peak_ready")
        shifted_ready = sem("shifted_ready")
        exp_ready = sem("exp_ready")
        total_ready = sem("total_ready")
        inverse_ready = sem("inverse_ready")
        alpha_ready = sem("alpha_ready")
        own_weighted = sem("own_weighted")
        next_weighted = sem("next_weighted")
        aux_weighted = sem("aux_weighted")
        pair_summed = sem("pair_summed")
        att_ready = sem("att_ready")
        last_pair_summed = sem("last_pair_summed")
        last_att_ready = sem("last_att_ready")
        last_attT_done = sem("last_attT_done")
        last_attT_hi_ready = sem("last_attT_hi_ready")
        last_attT_ready = sem("last_attT_ready")
        attT_done = sem("attT_done")
        attT_hi_ready = sem("attT_hi_ready")
        attT_ready = sem("attT_ready")
        resid_ready = sem("resid_ready")
        o_done = sem("o_done")
        out_ready = sem("out_ready")

        block = ctx.enter_context(nc.Block())

        def pipeline(eng, step, last):
            for t in range(SLOTS):
                step(0, t)
            with eng.Fori(1, TILES // SLOTS - 1) as i:
                for r in range(SLOTS):
                    step(i, r)
            for t in range(TILES - SLOTS, last + 1):
                step(*divmod(t, SLOTS))

        LAST = TILES - 1
        SHORT = (0, 1, LAST - 1, LAST)
        LOW_FIRST = (1, LAST)

        def own_taps(tiles):
            return tiles + sum(n < tiles for n in SHORT) if isinstance(tiles, int) else tiles + 2

        def next_taps(tiles):
            return 3 * tiles - own_taps(tiles) if isinstance(tiles, int) else tiles * 2 - 2

        def bcast_heads(row):
            return row.unsqueeze(2).to_broadcast([P, HEADS, HD])

        def by_head(row):
            return row.rearrange("p (h d) -> p h d", h=HEADS)

        @block.sync
        def _(sp):
            def load_x(u, slot):
                sp.dma_start(xT_raw[:, slot], xT[u]).then_inc(xT_in[slot], 16)

            sp.dma_start(xT_raw[:, 0], xT[0]).then_inc(xT_in[0], 16)
            for c in range(CK):
                sp.dma_start(products[:, c, :], wk[:, c, :]).then_inc(wk_in[c], 16)
            sp.dma_start(bk_raw, bk[0:2, :]).then_inc(small_in, 16)
            sp.dma_start(masks_raw, masks_in).then_inc(small_in, 16)
            load_x(1, 1)
            for c in range(CK):
                sp.dma_start(weighted[:, c, :], wq[:, c, :]).then_inc(wq_in[c], 16)
            sp.wait_ge(x_ready, 1)
            load_x(2, 0)
            for c in range(CK):
                sp.wait_ge(w_lo_ready, c + 1)
                sp.dma_start(products[:, c, :], wo[:, c, :]).then_inc(wo_in[c], 16)
            sp.dma_start(bq_rows[:], bq).then_inc(bq_in, 16)
            sp.dma_start(cond_raw[:], condT).then_inc(cond_in, 16)
            sp.dma_start(bv_rows, bv).then_inc(bv_in, 16)
            sp.dma_start(ident[:], ident_in).then_inc(late_in, 16)
            sp.dma_start(bo_rows[:], bo).then_inc(late_in, 16)
            sp.wait_ge(w_lo_ready, 2 * CK)
            sp.dma_start(weighted[:], wv).then_inc(wv_in, 16)
            sp.dma_start(bk_rows[:], bk).then_inc(bk_in, 16)
            sp.wait_ge(x_ready, 2)
            load_x(3, 1)
            sp.wait_ge(k_copied, 2)
            runs = P // BATCHES
            for b in range(BATCHES):
                sp.dma_start(halo[b * runs:(b + 1) * runs - 1, :],
                             keys[b * runs + 1:(b + 1) * runs, 1, :]).then_inc(halo_saved, 16)
            sp.dma_start(halo[runs - 1:P:runs, :], zeros_in).then_inc(halo_saved, 16)

            def step(i, r):
                t, static = i * SLOTS + r, isinstance(i, int)
                if not (static and t + 4 > TILES):
                    sp.wait_ge(x_ready, t + 3)
                    load_x(t + 4, r % 2)
                slot = (r + 1) % 2
                if static and t == LAST - 1:
                    sp.wait_ge(halo_saved, 16 * (BATCHES + 1))
                    sp.wait_ge(own_weighted, own_taps(t))
                    sp.wait_ge(next_weighted, next_taps(t - 1))
                    sp.dma_start(keys[:, (r + 3) % SLOTS, :], halo).then_inc(halo_in, 16)
                if not (static and t < 3):
                    sp.wait_ge(out_ready, t - 2)
                    sp.dma_start(out[:, t - 3, :], resid[:, slot, :]).then_inc(stored[slot], 16)
                if not (static and not 1 <= t <= TILES):
                    if not (static and t < 3):
                        sp.wait_ge(stored[slot], 16 * (2 * i + (r - 1) // 2))
                    sp.dma_start(resid[:, slot, :], x[:, t - 1, :]).then_inc(resid_in[slot], 16)

            pipeline(sp, step, TILES + 2)
            for s in range(2):
                sp.wait_ge(stored[s], 16 * (TILES // 2))

        @block.tensor
        def _(pe):
            def three_passes(dst, hi, lo, w_hi, w_lo, first, last):
                pe.matmul(dst, hi, w_hi, start=first, stop=False)
                pe.matmul(dst, hi, w_lo, start=False, stop=False)
                return pe.matmul(dst, lo, w_hi, start=False, stop=last)

            def keys_of(hi, lo, seq):
                pe.wait_ge(k_copied, seq)
                for n in range(2):
                    cols = slice(n * HALF, (n + 1) * HALF)
                    for c in range(CK):
                        mm = three_passes(ps_k[:, cols], hi[:, c, :], lo[:, c, :],
                                          wk_hi[:, c, cols], wk_lo[:, c, cols], c == 0, c == CK - 1)
                    mm.then_inc(k_half_done, 1)

            def biased_keys_of(dst, hi, lo, mask, arrives):
                for c in range(CK):
                    if arrives:
                        pe.wait_ge(w_lo_ready, c + 1)
                    for n in range(2):
                        cols = slice(n * HALF, (n + 1) * HALF)
                        three_passes(dst[:, cols], hi[:, c, :], lo[:, c, :],
                                     wk_hi[:, c, cols], wk_lo[:, c, cols], c == 0, False)
                if arrives:
                    pe.wait_ge(masks_ready, 1)
                    pe.wait_ge(bias_ready, 1)
                for n in range(2):
                    cols = slice(n * HALF, (n + 1) * HALF)
                    pe.matmul(dst[:, cols], masks[:, mask, :], bk_parts[:, cols],
                              start=False, stop=True).then_inc(k_half_done, 1)

            def queries_of(t, slot):
                if not (isinstance(t, int) and t == 0):
                    pe.wait_ge(q_used, t)
                for n in range(2):
                    cols = slice(n * HALF, (n + 1) * HALF)
                    for c in range(CK):
                        mm = three_passes(ps_q[:, cols], xT_hi[:, slot, c, :], xT_lo[:, slot, c, :],
                                          wq_hi[:, c, cols], wq_lo[:, c, cols], c == 0, c == CK - 1)
                mm.then_inc(q_done, 1)

            def turn_last():
                pe.wait_ge(attT_ready, LAST)
                for n in range(2):
                    pe.wait_ge(last_att_ready, n + 1)
                    for c in range(n * HK // 2, (n + 1) * HK // 2):
                        mm = pe.transpose(ps_t[:, c, :], att[:, c * P:(c + 1) * P], ident[:])
                    mm.then_inc(last_attT_done, 1)

            def last_output():
                pe.wait_ge(out_ready, LAST)
                for c in range(HK):
                    if c % (HK // 2) == 0:
                        pe.wait_ge(last_attT_ready, 1 + 2 * c // HK)
                    mm = three_passes(ps_o[:], attT_hi[:, c, :], attT_lo[:, c, :],
                                      wo_hi[:, c, :], wo_lo[:, c, :], c == 0, c == HK - 1)
                mm.then_inc(o_done, 1)

            def turn(n):
                pe.wait_ge(att_ready, n + 1)
                if isinstance(n, int) and n == 0:
                    pe.wait_ge(late_in, 16 * 2)
                if not (isinstance(n, int) and n == 0):
                    pe.wait_ge(attT_ready, n)
                for c in range(HK):
                    mm = pe.transpose(ps_t[:, c, :], att[:, c * P:(c + 1) * P], ident[:])
                mm.then_inc(attT_done, 1)

            def output_of(n):
                pe.wait_ge(attT_ready, n + 1)
                if not (isinstance(n, int) and n == 0):
                    pe.wait_ge(out_ready, n)
                for c in range(HK):
                    mm = three_passes(ps_o[:], attT_hi[:, c, :], attT_lo[:, c, :],
                                      wo_hi[:, c, :], wo_lo[:, c, :], c == 0, c == HK - 1)
                mm.then_inc(o_done, 1)

            pe.wait_ge(x_ready, 1)
            biased_keys_of(ps_k, xT_hi[:, 0], xT_lo[:, 0], 1, True)
            pe.wait_ge(x_ready, 2)
            biased_keys_of(ps_q, xT_hi[:, 1], xT_lo[:, 1], 0, False)
            pe.wait_ge(x_ready, 3)
            pe.wait_ge(k_copied, 1)
            biased_keys_of(ps_k, xT_hi[:, 2], xT_lo[:, 2], 0, False)
            pe.wait_ge(w_lo_ready, 2 * CK)

            def values_of_aux():
                pe.wait_ge(wv_in, 16)
                for n in range(2):
                    cols = slice(n * HALF, (n + 1) * HALF)
                    dst = ps_t.rearrange("p c n -> p (c n)")[:, cols]
                    for c in range(CK):
                        mm = pe.matmul(dst, cond_raw[:, c, :], weighted[:, c, cols], start=(c == 0), stop=(c == CK - 1))
                mm.then_inc(av_done, 1)

            def step(i, r):
                t, static = i * SLOTS + r, isinstance(i, int)
                if not (static and (t == 0 or t >= LAST)):
                    pe.wait_ge(x_ready, t + 3)
                    slot = (r + 2) % SLOTS
                    keys_of(xT_hi[:, slot], xT_lo[:, slot], t + 3)
                if static and t == LAST:
                    queries_of(t, (r + 1) % SLOTS)
                if static and t == LAST + 2:
                    turn_last()
                elif not (static and t < 2):
                    turn(t - 2)
                if not (static and t >= LAST):
                    if static and t == 0:
                        pe.wait_ge(k_copied, 2)
                    queries_of(t, (r + 1) % SLOTS)
                if static and t == 0:
                    pe.wait_ge(cond_ready, 1)
                    pe.wait_ge(k_copied, 3)
                    biased_keys_of(ps_k, cond_hi, cond_lo, 0, False)
                    values_of_aux()
                if static and t == 2:
                    pe.wait_ge(w_lo_ready, 3 * CK)
                if static and t == LAST + 2:
                    last_output()
                elif not (static and t < 2):
                    output_of(t - 2)

            pipeline(pe, step, TILES + 1)

        @block.scalar
        def _(act):
            def copy(dst, src):
                return act.activation(dst, src, ACT.Copy)

            def x_high(u, slot, count):
                act.wait_ge(xT_in[slot % 2], 16 * count)
                copy(xT_hi[:, slot], xT_raw[:, slot % 2]).then_inc(x_hi_ready, 1)

            def keys_out(dst, seq, src=ps_k):
                for n in range(2):
                    cols = slice(n * HALF, (n + 1) * HALF)
                    act.wait_ge(k_half_done, 2 * seq + n + 1)
                    ins = copy(dst[:, cols], src[:, cols])
                ins.then_inc(k_copied, 1)

            x_high(0, 0, 1)
            for c in range(CK):
                act.wait_ge(wk_in[c], 16)
                copy(wk_hi[:, c, :], products[:, c, :]).then_inc(w_hi_ready, 1)
            act.wait_ge(small_in, 32)
            copy(masks[:], masks_raw).then_inc(masks_ready, 1)
            copy(bk_high.bitcast(F32R), bk_raw).then_inc(bias_hi_ready, 1)
            x_high(1, 1, 1)

            def wq_high(c):
                act.wait_ge(wq_in[c], 16)
                copy(wq_hi[:, c, :], weighted[:, c, :]).then_inc(w_hi_ready, 1)

            def wo_high(c):
                act.wait_ge(wo_in[c], 16)
                copy(wo_hi[:, 2 * c:2 * c + 2, :],
                     products[:, c, :].rearrange("p (c n) -> p c n", c=2)).then_inc(w_hi_ready, 1)

            wq_high(0)
            keys_out(keys[:, 0], 0)
            wq_high(1)
            wq_high(2)
            x_high(2, 2, 2)
            wq_high(3)
            keys_out(keys[:, 1], 1, ps_q)
            wo_high(0)
            wo_high(1)
            act.wait_ge(bias_ready, 1)
            keys_out(keys[:, 2], 2)
            wo_high(2)
            wo_high(3)
            act.wait_ge(cond_in, 16)
            copy(cond_hi, cond_raw[:]).then_inc(cond_hi_ready, 1)

            def weigh_next(t, r):
                act.wait_ge(alpha_ready, t + 1)
                if not (isinstance(t, int) and t == 0):
                    act.wait_ge(att_ready, t)
                for j in (2,) if isinstance(t, int) and t in SHORT else (1, 2):
                    for h in range(HEADS):
                        cols = slice(h * HD, (h + 1) * HD)
                        ins = act.activation(weighted[:, j, cols], keys[:, (r + j) % SLOTS, cols], ACT.Copy,
                                             scale=alpha[:, j, h:h + 1])
                    ins.then_inc(next_weighted, 1)

            def exp_of(t):
                act.wait_ge(shifted_ready, t + 1)
                act.activation(expd[:], shifted[:], ACT.Exp, scale=SCALE).then_inc(exp_ready, 1)

            def step(i, r):
                t, static = i * SLOTS + r, isinstance(i, int)
                if not (static and (not 1 <= t <= LAST or t - 1 in LOW_FIRST)):
                    exp_of(t - 1)
                if not (static and t >= LAST):
                    if not (static and t < 2):
                        act.wait_ge(own_weighted, own_taps(t - 1))
                    if static and t == 0:
                        keys_out(aux_key, 3)
                    else:
                        if static and t == SLOTS - 1:
                            act.wait_ge(halo_saved, 16 * (BATCHES + 1))
                        keys_out(keys[:, (r + 2) % SLOTS], t + 3)
                if static and t == LAST + 2:
                    for n in range(2):
                        act.wait_ge(last_attT_done, n + 1)
                        if n == 0:
                            act.wait_ge(o_done, LAST)
                        half = slice(n * HK // 2, (n + 1) * HK // 2)
                        copy(attT_hi[:, half], ps_t[:, half]).then_inc(last_attT_hi_ready, 1)
                elif not (static and t < 2):
                    act.wait_ge(attT_done, t - 1)
                    if not (static and t < 3):
                        act.wait_ge(o_done, t - 2)
                    copy(attT_hi[:], ps_t[:]).then_inc(attT_hi_ready, 1)
                if static and t - 1 in LOW_FIRST:
                    exp_of(t - 1)
                if not (static and t + 3 > TILES):
                    if static and t == 1:
                        act.wait_ge(k_half_done, 2)
                    if not (static and t < 2):
                        act.wait_ge(q_done, t - 1)
                    x_high(t + 3, (r + 3) % SLOTS, 2 * i + (r + 3) // 2 + 1)
                if not (static and not 1 <= t <= TILES):
                    weigh_next(t - 1, (r - 1) % SLOTS)

            pipeline(act, step, TILES + 1)

        @block.vector
        def _(dve):
            dve.memset(low_row[:], -1.0).then_inc(rows_set, 1)
            dve.wait_ge(rows_set, 1)
            dve.memset(low_row[0:1, :], 0.0).then_inc(rows_set, 1)

            def low(dst, raw, hi):
                return dve.tensor_tensor(dst, raw, hi.bitcast(F32), ALU.subtract)

            def x_low(u, slot):
                dve.wait_ge(x_hi_ready, u + 1)
                low(xT_lo[:, slot], xT_raw[:, slot % 2], xT_hi[:, slot]).then_inc(x_ready, 1)

            def bias_parts():
                dve.wait_ge(bias_hi_ready, 1)
                dve.wait_ge(rows_set, 2)
                dve.scalar_tensor_tensor(bk_parts[:], bk_high, low_row[:, 0:1], bk_raw,
                                         ALU.mult, ALU.add).then_inc(bias_ready, 1)

            x_low(0, 0)
            for c in range(CK):
                dve.wait_ge(w_hi_ready, c + 1)
                low(wk_lo[:, c, :], products[:, c, :], wk_hi[:, c, :]).then_inc(w_lo_ready, 1)
            bias_parts()
            x_low(1, 1)
            for c in range(CK):
                if c == 3:
                    x_low(2, 2)
                dve.wait_ge(w_hi_ready, CK + c + 1)
                low(wq_lo[:, c, :], weighted[:, c, :], wq_hi[:, c, :]).then_inc(w_lo_ready, 1)
            for c in range(CK):
                dve.wait_ge(w_hi_ready, 2 * CK + c + 1)
                low(wo_lo[:, 2 * c:2 * c + 2, :], products[:, c, :].rearrange("p (c n) -> p c n", c=2),
                    wo_hi[:, 2 * c:2 * c + 2, :]).then_inc(w_lo_ready, 1)
            dve.wait_ge(cond_hi_ready, 1)
            low(cond_lo, cond_raw[:], cond_hi).then_inc(cond_ready, 1)

            def scores_of(t, r):
                dve.wait_ge(q_done, t + 1)
                if isinstance(t, int) and t == 0:
                    dve.wait_ge(bq_in, 16)
                dve.tensor_tensor(ps_q[:], ps_q[:], bq_rows[:], ALU.add).then_inc(q_biased, 1)
                dve.wait_ge(q_biased, t + 1)
                if isinstance(t, int) and t == 0:
                    dve.wait_ge(k_copied, 3)
                    dve.wait_ge(w_lo_ready, 3 * CK)
                elif isinstance(t, int) and t == LAST:
                    dve.wait_ge(halo_in, 16)
                    dve.wait_ge(k_ready, t - 1)
                else:
                    dve.wait_ge(k_ready, t)
                for j in range(TAPS):
                    if j == AUX and isinstance(t, int) and t == 0:
                        dve.wait_ge(k_copied, 4)
                    k = aux_key[:] if j == AUX else keys[:, (r + j) % SLOTS, :]
                    ins = dve.tensor_tensor(products[:, j, :], ps_q[:], k, ALU.mult)
                ins.then_inc(q_used, 1)
                dve.wait_ge(q_used, t + 1)
                dve.tensor_reduce(scores[:], products.rearrange("p j (h d) -> p (j h) d", h=HEADS), AX.X,
                                  ALU.add).then_inc(scores_ready, 1)
                dve.wait_ge(scores_ready, t + 1)
                dve.tensor_reduce(peak[:], scores.rearrange("p j h -> p h j"), AX.X, ALU.max).then_inc(peak_ready, 1)
                dve.wait_ge(peak_ready, t + 1)
                dve.tensor_tensor(shifted[:], scores[:], peak[:].unsqueeze(1).to_broadcast([P, TAPS, HEADS]),
                                  ALU.subtract).then_inc(shifted_ready, 1)

            def weigh(t, r):
                dve.wait_ge(exp_ready, t + 1)
                dve.tensor_reduce(total[:], expd.rearrange("p j h -> p h j"), AX.X, ALU.add).then_inc(total_ready, 1)
                dve.wait_ge(total_ready, t + 1)
                dve.reciprocal(inverse[:], total[:]).then_inc(inverse_ready, 1)
                dve.wait_ge(inverse_ready, t + 1)
                if not (isinstance(t, int) and t == 0):
                    dve.wait_ge(aux_weighted, t)
                    dve.wait_ge(next_weighted, next_taps(t))
                dve.tensor_tensor(alpha[:], expd[:], inverse[:].unsqueeze(1).to_broadcast([P, TAPS, HEADS]),
                                  ALU.mult).then_inc(alpha_ready, 1)
                dve.wait_ge(alpha_ready, t + 1)
                if not (isinstance(t, int) and t == 0):
                    dve.wait_ge(att_ready, t)
                if isinstance(t, int) and t == 0:
                    dve.wait_ge(av_done, 1)
                for j in (0, 1) if isinstance(t, int) and t in SHORT else (0,):
                    dve.tensor_tensor(by_head(weighted[:, j, :]), by_head(keys[:, (r + j) % SLOTS, :]),
                                      bcast_heads(alpha[:, j, :]), ALU.mult).then_inc(own_weighted, 1)

            def sum_last():
                dve.wait_ge(own_weighted, own_taps(TILES))
                dve.wait_ge(aux_weighted, TILES)
                dve.tensor_tensor(weighted[:, 0, :], weighted[:, 0, :], weighted[:, AUX, :],
                                  ALU.add).then_inc(last_pair_summed, 1)
                dve.wait_ge(next_weighted, next_taps(TILES))
                dve.tensor_tensor(weighted[:, 1, :], weighted[:, 1, :], weighted[:, 2, :],
                                  ALU.add).then_inc(last_pair_summed, 1)
                dve.wait_ge(last_pair_summed, 2)
                dve.wait_ge(attT_done, LAST)
                for n in range(2):
                    cols = slice(n * HALF, (n + 1) * HALF)
                    dve.tensor_tensor(att[:, cols], weighted[:, 0, cols], weighted[:, 1, cols],
                                      ALU.add).then_inc(last_att_ready, 1)

            def low_last_attT():
                dve.wait_ge(o_done, LAST)
                for n in range(2):
                    half = slice(n * HK // 2, (n + 1) * HK // 2)
                    dve.wait_ge(last_attT_hi_ready, n + 1)
                    dve.tensor_tensor(attT_lo[:, half], ps_t[:, half], attT_hi[:, half].bitcast(F32),
                                      ALU.subtract).then_inc(last_attT_ready, 1)

            def low_attT(n):
                dve.wait_ge(attT_hi_ready, n + 1)
                if not (isinstance(n, int) and n == 0):
                    dve.wait_ge(o_done, n)
                dve.tensor_tensor(attT_lo[:], ps_t[:], attT_hi[:].bitcast(F32), ALU.subtract).then_inc(attT_ready, 1)

            def add_residual(n, slot):
                dve.wait_ge(o_done, n + 1)
                dve.wait_ge(resid_ready, n + 1)
                dve.tensor_tensor(resid[:, slot, :], ps_o[:], resid[:, slot, :], ALU.add).then_inc(out_ready, 1)

            def step(i, r):
                t, static = i * SLOTS + r, isinstance(i, int)
                if not (static and (t == 0 or t + 3 > TILES)):
                    x_low(t + 3, (r + 3) % SLOTS)
                if not (static and t > LAST):
                    scores_of(t, r)
                if static and t == 0:
                    x_low(3, 3)
                    dve.wait_ge(av_done, 1)
                    dve.wait_ge(bv_in, 16)
                    dve.tensor_tensor(aux_value[:], ps_t.rearrange("p c n -> p (c n)"), bv_rows,
                                      ALU.add).then_inc(av_ready, 1)
                if static and t == LAST + 2:
                    low_last_attT()
                if static and t in LOW_FIRST:
                    low_attT(t - 1)
                if not (static and not 2 <= t <= LAST + 2):
                    add_residual(t - 2, r % 2)
                if not (static and t > LAST):
                    weigh(t, r)
                if not (static and (not 1 <= t < LAST or t in LOW_FIRST)):
                    low_attT(t - 1)
                if static and t == LAST:
                    sum_last()

            pipeline(dve, step, TILES + 1)

        @block.gpsimd
        def _(pool):
            def sum_values(t):
                first = isinstance(t, int) and t == 0
                pool.wait_ge(aux_weighted, t + 1)
                pool.wait_ge(own_weighted, own_taps(t + 1))
                pool.tensor_tensor(weighted[:, 0, :], weighted[:, 0, :], weighted[:, AUX, :],
                                   ALU.add).then_inc(pair_summed, 1)
                pool.wait_ge(next_weighted, next_taps(t + 1))
                pool.tensor_tensor(weighted[:, 1, :], weighted[:, 1, :], weighted[:, 2, :],
                                   ALU.add).then_inc(pair_summed, 1)
                pool.wait_ge(pair_summed, 2 * t + 2)
                if not first:
                    pool.wait_ge(attT_done, t)
                pool.tensor_tensor(att[:], weighted[:, 0, :], weighted[:, 1, :], ALU.add).then_inc(att_ready, 1)

            def step(i, r):
                t, static = i * SLOTS + r, isinstance(i, int)
                if static and t == 0:
                    pool.wait_ge(av_ready, 1)
                    pool.wait_ge(bk_in, 16)
                if not (static and not 1 <= t <= TILES):
                    pool.wait_ge(alpha_ready, t)
                    if not (static and t == 1):
                        pool.wait_ge(att_ready, t - 1)
                    pool.tensor_tensor(by_head(weighted[:, AUX, :]), by_head(aux_value[:]),
                                       bcast_heads(alpha[:, AUX, :]), ALU.mult).then_inc(aux_weighted, 1)
                if not (static and not 1 <= t < LAST):
                    pool.wait_ge(k_copied, t + 4)
                    slot = (r + 2) % SLOTS
                    pool.tensor_tensor(keys[:, slot, :], keys[:, slot, :], bk_rows[:], ALU.add).then_inc(k_ready, 1)
                if not (static and not 1 <= t <= LAST):
                    sum_values(t - 1)
                if not (static and not 2 <= t <= TILES + 1):
                    slot = r % 2
                    pool.wait_ge(resid_in[slot], 16 * (2 * i + r // 2))
                    pool.tensor_tensor(resid[:, slot, :], resid[:, slot, :], bo_rows[:], ALU.add).then_inc(resid_ready, 1)

            pool.wait_ge(late_in, 16 * 2)
            pipeline(pool, step, TILES + 1)


def kernel(**inputs):
    import numpy as np
    import concourse.bacc as bacc
    from concourse import mybir as mb
    from concourse.bass_utils import run_bass_kernel_spmd as run

    x = np.asarray(inputs["x"])
    batches, length, _ = x.shape
    runs = P // batches
    padded = np.pad(x, ((0, 0), (1, 1), (0, 0)))
    tiles = [padded[:, u:u + length:TILES, :][:, :runs].reshape(P, CK, P).transpose(2, 1, 0) for u in range(TILES + 1)]
    cond = np.repeat(np.asarray(inputs["cond_1024"]), runs, axis=0).reshape(P, CK, P).transpose(2, 1, 0)

    def weight(name, chunks):
        w = np.asarray(inputs[name])
        return w.reshape(chunks, P, w.shape[1]).transpose(1, 0, 2)

    def rows(name):
        b = np.asarray(inputs[name])
        return np.broadcast_to(b, (P, b.size))

    masks = np.ones((2, 2, P), np.float32)
    masks[:, 1, 0::runs] = 0.0
    arrays = {
        "xT": np.stack(tiles),
        "x_tokens": x.reshape(P, TILES, C),
        "condT": cond,
        "wq": weight("L0_cond_WQ_w", CK),
        "wk": weight("L0_cond_WK_w", CK),
        "wv": weight("L0_cond_WV_w", CK),
        "wo": weight("L0_cond_WO_w", HK).reshape(P, CK, CH),
        "bq": rows("L0_cond_WQ_b"),
        "bk": rows("L0_cond_WK_b"),
        "bv": rows("L0_cond_WV_b"),
        "bo": rows("L0_cond_WO_b"),
        "ident": np.eye(P, dtype=np.float32),
        "masks": masks,
        "zeros": np.zeros((batches, CH), np.float32),
    }
    arrays = {k: np.ascontiguousarray(v) for k, v in arrays.items()}
    nc = bacc.Bacc("TRN2", target_bir_lowering=False, num_devices=1)
    args = [nc.dram_tensor("in_" + k, v.shape, mb.dt.from_np(v.dtype), kind="ExternalInput").ap() for k, v in arrays.items()]
    xT, x_ap, condT, wq, wk, wv, wo, bq, bk, bv, bo, ident, masks_ap, zeros = args
    out = nc.dram_tensor("out", (P, TILES, C), mb.dt.float32, kind="ExternalOutput").ap()
    build(nc, xT, x_ap, condT, wq, wk, wv, wo, bq, bk, bv, bo, ident, masks_ap, zeros, out)
    got = run(nc, [{"in_" + k: v for k, v in arrays.items()}], core_ids=[0])
    return got.results[0]["out"].reshape(batches, length, C)
```
